# Optimizing a Trainium2 kernel written in Bass

```python
import numpy as np
import jax
import jax.numpy as jnp

def _softmax(x, axis=-1):
    return jax.nn.softmax(x, axis=axis)

def _gelu(x):
    return jax.nn.gelu(x, approximate=True)

def _silu(x):
    return jax.nn.silu(x)

def _sigmoid(x):
    return jax.nn.sigmoid(x)

def _layernorm(x, axis=-1, eps=1e-05):
    m = jnp.mean(x, axis=axis, keepdims=True)
    v = jnp.var(x, axis=axis, keepdims=True)
    return (x - m) / jnp.sqrt(v + eps)

def _scatter_add(tgt, idx, src, axis=0):
    return tgt.at[idx].add(src)

def _segment_sum(src, seg, n):
    return jax.ops.segment_sum(src, seg, n)
kernel_name = 'mk_gnn_resnorm_d2_gnn_r8_95a7a4'

def setup_inputs(seed: int=0):
    np.random.seed(seed)
    _w = jnp.asarray

    def _rec_inputs():
        import jax
        import jax.numpy as jnp
        _gk = jax.random.key(seed)
        x = -0.0003713 + 1 * jax.random.normal(jax.random.fold_in(_gk, 1), (12500, 128), jnp.float32)
        _s = jax.random.randint(jax.random.fold_in(_gk, 2), (200000,), 0, 12500, jnp.int32)
        _d = jax.random.randint(jax.random.fold_in(_gk, 3), (200000,), 0, 12500, jnp.int32)
        _loop = jnp.arange(12500, dtype=jnp.int32)
        src = jnp.concatenate([_s, _d, _loop])
        dst = jnp.concatenate([_d, _s, _loop])
        _o = jnp.argsort(dst, stable=True)
        src = src[_o]
        dst = dst[_o]
        edge_attr_64 = -7.08334e-05 + 0.999895 * jax.random.normal(jax.random.fold_in(_gk, 12), (412500, 64), jnp.float32)
        edge_weight = jax.random.uniform(jax.random.fold_in(_gk, 14), (412500,), jnp.float32, 0.0, 1)
        return (x, src, dst, edge_attr_64, edge_weight)
    x, src, dst, edge_attr_64, edge_weight = _rec_inputs()

    def _L0_gnn_setup():
        import jax, jax.numpy as jnp
        import numpy as np
        N_NODES = 12500
        N_EDGES = 200000
        EMB = 128
        key = jax.random.key(seed)
        k1, k2, k3, k4, k5, k6 = jax.random.split(key, 6)
        embeddings = jax.random.normal(k1, (N_NODES, EMB), dtype=jnp.float32)
        edge_row = jax.random.randint(k2, (N_EDGES,), 0, N_NODES, dtype=jnp.int32)
        edge_col = jax.random.randint(k3, (N_EDGES,), 0, N_NODES, dtype=jnp.int32)
        edge_val = jax.random.uniform(k4, (N_EDGES,), dtype=jnp.float32)
        W1 = jax.random.normal(k5, (EMB, EMB), dtype=jnp.float32) * (1.0 / np.sqrt(EMB))
        W2 = jax.random.normal(k6, (EMB, EMB), dtype=jnp.float32) * (1.0 / np.sqrt(EMB))
        return {'embeddings': embeddings, 'edge_row': edge_row, 'edge_col': edge_col, 'edge_val': edge_val, 'W1': W1, 'W2': W2}
    _L0_gnn_all = _L0_gnn_setup()
    _L0_gnn_in = {k: v for k, v in _L0_gnn_all.items() if k in ('W1', 'W2')}
    del _L0_gnn_all

    def _L1_gnn_setup():
        import jax, jax.numpy as jnp
        import numpy as np
        N, E, D, H, ED = (6250, 75000, 128, 8, 64)
        DH = D // H
        SCALE = DH ** (-0.5)
        key = jax.random.key(seed)
        ks = jax.random.split(key, 12)
        s = 1.0 / np.sqrt(D)
        se = 1.0 / np.sqrt(ED)
        return {'x': jax.random.normal(ks[0], (N, D), jnp.float32), 'edge_attr': jax.random.normal(ks[1], (E, ED), jnp.float32), 'Wq': jax.random.uniform(ks[2], (D, D), jnp.float32, -s, s), 'bq': jnp.zeros((D,), jnp.float32), 'Wk': jax.random.uniform(ks[3], (D, D), jnp.float32, -s, s), 'bk': jnp.zeros((D,), jnp.float32), 'Wv': jax.random.uniform(ks[4], (D, D), jnp.float32, -s, s), 'bv': jnp.zeros((D,), jnp.float32), 'We': jax.random.uniform(ks[5], (ED, D), jnp.float32, -se, se), 'be': jnp.zeros((D,), jnp.float32), 'Wo': jax.random.uniform(ks[6], (D, D), jnp.float32, -s, s), 'bo': jnp.zeros((D,), jnp.float32), 'edge_index': jax.random.randint(ks[7], (2, E), 0, N, jnp.int32)}
    _L1_gnn_all = _L1_gnn_setup()
    _L1_gnn_in = {k: v for k, v in _L1_gnn_all.items() if k in ('Wq', 'bq', 'Wk', 'bk', 'Wv', 'bv', 'We', 'be', 'Wo', 'bo')}
    del _L1_gnn_all
    return {'x': x, 'src': src, 'dst': dst, 'edge_attr_64': edge_attr_64, 'edge_weight': edge_weight, 'L0_gnn_W1': _L0_gnn_in['W1'], 'L0_gnn_W2': _L0_gnn_in['W2'], 'L1_gnn_Wq': _L1_gnn_in['Wq'], 'L1_gnn_bq': _L1_gnn_in['bq'], 'L1_gnn_Wk': _L1_gnn_in['Wk'], 'L1_gnn_bk': _L1_gnn_in['bk'], 'L1_gnn_Wv': _L1_gnn_in['Wv'], 'L1_gnn_bv': _L1_gnn_in['bv'], 'L1_gnn_We': _L1_gnn_in['We'], 'L1_gnn_be': _L1_gnn_in['be'], 'L1_gnn_Wo': _L1_gnn_in['Wo'], 'L1_gnn_bo': _L1_gnn_in['bo']}

def reference(x, src, dst, edge_attr_64, edge_weight, L0_gnn_W1, L0_gnn_W2, L1_gnn_Wq, L1_gnn_bq, L1_gnn_Wk, L1_gnn_bk, L1_gnn_Wv, L1_gnn_bv, L1_gnn_We, L1_gnn_be, L1_gnn_Wo, L1_gnn_bo):
    import jax
    import jax.numpy as jnp

    def _L0_gnn_ref(embeddings, edge_row, edge_col, edge_val, W1, W2):
        import jax, jax.numpy as jnp
        import numpy as np
        N_NODES = 12500
        N_EDGES = 200000
        EMB = 128
        gathered = embeddings[edge_col] * edge_val[:, None]
        relevant = jax.ops.segment_sum(gathered, edge_row, num_segments=N_NODES)
        non_interactive = relevant @ W1
        interactive = relevant * embeddings @ W2
        return non_interactive + interactive

    def _L1_gnn_ref(x, edge_attr, Wq, bq, Wk, bk, Wv, bv, We, be, Wo, bo, edge_index):
        import jax, jax.numpy as jnp
        import numpy as np
        N, E, D, H, ED = (6250, 75000, 128, 8, 64)
        DH = D // H
        SCALE = DH ** (-0.5)
        src, dst = (edge_index[0], edge_index[1])
        n = x.shape[0]
        q = (x @ Wq + bq).reshape(n, H, DH)
        k = (x @ Wk + bk).reshape(n, H, DH)
        v = (x @ Wv + bv).reshape(n, H, DH)
        e = (edge_attr @ We + be).reshape(-1, H, DH)
        q_dst = q[dst]
        k_src = k[src]
        logits = ((q_dst * k_src).sum(-1) + (q_dst * e).sum(-1)) * SCALE
        m = jax.ops.segment_max(logits, dst, num_segments=n)
        ex = jnp.exp(logits - m[dst])
        denom = jax.ops.segment_sum(ex, dst, num_segments=n)
        attn = ex / denom[dst]
        messages = attn[..., None] * v[src]
        out = jax.ops.segment_sum(messages, dst, num_segments=n)
        out = out.reshape(n, D)
        return out @ Wo + bo
    edge_index = jnp.stack([src, dst])
    x = _layernorm(x + _L0_gnn_ref(x, src, dst, edge_weight, L0_gnn_W1, L0_gnn_W2), axis=-1)
    x = _layernorm(x + _L1_gnn_ref(x, edge_attr_64, L1_gnn_Wq, L1_gnn_bq, L1_gnn_Wk, L1_gnn_bk, L1_gnn_Wv, L1_gnn_bv, L1_gnn_We, L1_gnn_be, L1_gnn_Wo, L1_gnn_bo, edge_index), axis=-1)
    return x

_drawn_inputs = setup_inputs


def setup_inputs(seed=0):
    import zlib

    import numpy as np

    out = dict(_drawn_inputs(seed))
    spreads = {'L1_gnn_bq': (0.0, 0.8),
     'L1_gnn_bk': (0.0, 0.8),
     'L1_gnn_bv': (0.0, 0.1),
     'L1_gnn_be': (0.0, 0.8),
     'L1_gnn_bo': (0.0, 0.1)}
    factors = {'edge_attr_64': 2.721, 'L1_gnn_We': 2.712}
    for name, (base, spread) in spreads.items():
        noise = np.random.default_rng([zlib.crc32(name.encode()), seed]).standard_normal(out[name].shape)
        drawn = base * np.exp(spread * noise) if base else spread * noise
        out[name] = jnp.asarray(drawn.astype(out[name].dtype))
    for name, factor in factors.items():
        out[name] = (out[name] * factor).astype(out[name].dtype)
    return out
```

```python
from contextlib import ExitStack

import concourse.bass as bass
from concourse import mybir

F32 = mybir.dt.float32
I32 = mybir.dt.int32
BF16 = mybir.dt.bfloat16
ALU = mybir.AluOpType
ACT = mybir.ActivationFunctionType
AX_X = mybir.AxisListType.X

P = 128
G = 8
REPLICAS = 4
BIG = 1.0e30
EPS = 1.0e-5
NB = 4 * P


def load_starts(eng, regs, words, top):
    eng.load(regs, words)
    return [eng.snap(r, min_val=0, max_val=top) for r in regs]


class Step:

    def __init__(self, u, k, unroll):
        self.u, self.k, self.unroll = u, k, unroll

    def plus(self, d):
        return Step(self.u, self.k + d, self.unroll)

    @property
    def g(self):
        return self.u * self.unroll + self.k

    def before(self, n):
        return not isinstance(self.u, int) or self.k < n

    def turn(self, ring):
        return self.k % ring

    def uses(self, ring):
        return self.u * (self.unroll // ring) + (self.k // ring + 1)


def wait(eng, sem, value):
    if isinstance(value, int) and value <= 0:
        return
    eng.wait_ge(sem, value)


def wait_alone(eng, sem, value, passed):
    wait(eng, sem, value)
    eng.sem_inc(passed, 1)


def steps(eng, n, unroll, head, tail, body):
    loops = (n - head - tail) // unroll
    first = head // unroll
    for k in range(head):
        body(Step(0, k, unroll))
    with eng.Fori(first, first + loops) as u:
        for k in range(unroll):
            body(Step(u, k, unroll))
    for k in range(head + loops * unroll, n):
        body(Step(0, k, unroll))


def build_gnn(nc, x, src, dst, edge_attr, edge_weight, W1, W2, Wq, bq, Wk, bk, Wv, bv, We, be, Wo, bo, out):
    N, D = x.shape
    E, ED = edge_attr.shape
    H = 8
    DH = D // H
    SCALE = float(DH) ** -0.5
    assert D == P and ED == 64 and N >= NB
    NG = -(-E // (G * P))
    T = NG * G
    NC = -(-T // P)
    TP = NC * P
    PAD_DST = N + P
    FULL_ROWS = E // P
    TAIL = E - FULL_ROWS * P
    LAST = N - P
    GP = G * P
    GH = G * H

    dst_pad = nc.dram_tensor("dst_pad", (1 + TP * P + 1,), I32).ap()
    src_flat = nc.dram_tensor("src_flat", (TP * P,), F32).ap()
    rel_flat = nc.dram_tensor("rel_flat", (TP * P,), F32).ap()
    marks = nc.dram_tensor("marks", (TP, 4, P), F32).ap()
    whole = nc.dram_tensor("whole", (2, TP), F32).ap()
    src_cols = nc.dram_tensor("src_cols", (P, TP), I32).ap()
    starts = nc.dram_tensor("starts", (TP,), I32).ap()
    firsts = nc.dram_tensor("firsts", (TP,), I32).ap()
    rel_sum = [nc.dram_tensor(f"rel_sum{r}", (N + P, D), F32).ap() for r in range(REPLICAS)]
    x1_rows = nc.dram_tensor("x1_rows", (N, D), F32).ap()
    q_rows = nc.dram_tensor("q_rows", (N, D), F32).ap()
    kv_rows = nc.dram_tensor("kv_rows", (N, 2 * D), F32).ap()

    with ExitStack() as outer:
        passed = outer.enter_context(nc.semaphore("passed"))
        def keep(name, shape, dt=F32):
            return outer.enter_context(nc.sbuf_tensor(name, shape, dt))

        iota_i = keep("iota_i", [P, P], I32)
        iota_n = keep("iota_n", [P, P])
        part_i = keep("part_i", [P, 1], I32)
        part = keep("part", [P, 1])
        neg_part = keep("neg_part", [P, 1])
        dump_row = keep("dump_row", [P, 1])
        ident = keep("ident", [P, P])
        later = keep("later", [P, P])
        neg_rel = keep("neg_rel", [P, TP], BF16)

        with ExitStack() as mid:
            def sb(name, shape, dt=F32):
                return mid.enter_context(nc.sbuf_tensor(name, shape, dt))

            src_col = sb("src_col", [P, TP])
            w_col = sb("w_col", [P, TP])
            prepare(nc, locals())
            neighbours(nc, locals())
        nodes_one(nc, locals())
        attention_and_out(nc, locals())


def prepare(nc, e):
    N, E, NC, TP = e["N"], e["E"], e["NC"], e["TP"]
    FULL_ROWS, TAIL, PAD_DST, LAST = e["FULL_ROWS"], e["TAIL"], e["PAD_DST"], e["LAST"]
    src, dst, edge_weight = e["src"], e["dst"], e["edge_weight"]
    dst_pad, src_flat, rel_flat, marks, whole = e["dst_pad"], e["src_flat"], e["rel_flat"], e["marks"], e["whole"]
    src_cols, starts, firsts, rel_sum = e["src_cols"], e["starts"], e["firsts"], e["rel_sum"]
    iota_i, iota_n, part_i, part, neg_part = e["iota_i"], e["iota_n"], e["part_i"], e["part"], e["neg_part"]
    ident, later, neg_rel, src_col, w_col = e["ident"], e["later"], e["neg_rel"], e["src_col"], e["w_col"]
    dump_row = e["dump_row"]
    FC = FULL_ROWS // P
    FR = FULL_ROWS - FC * P
    ZW = (N + P) * P // P // 4

    with ExitStack() as ctx:
        def sb(name, shape, dt=F32):
            return ctx.enter_context(nc.sbuf_tensor(name, shape, dt))

        def sem(name):
            return ctx.enter_context(nc.semaphore(name))

        src_t = sb("src_t", [P, NC, P], I32)
        dst_t = sb("dst_t", [P, NC, P], I32)
        prev_t = sb("prev_t", [P, NC, P], I32)
        next_t = sb("next_t", [P, NC, P], I32)
        w_t = sb("w_t", [P, NC, P])
        srcf_t = sb("srcf_t", [P, NC, P])
        nrel_t = sb("nrel_t", [P, NC, P])
        start_t = sb("start_t", [P, NC, 1])
        start_ti = sb("start_ti", [P, NC, 1], I32)
        mark_t = sb("mark_t", [P, 4, NC, P])
        edge_of = sb("edge_of", [1, 2], I32)
        zeros = sb("zeros", [P, ZW])
        psum = [ctx.enter_context(nc.psum_tensor(f"turn{i}", [P, 512], F32)) for i in range(2)]
        filled, loaded, padded, shifted, prep_stored = (sem(n) for n in (
            "filled", "loaded", "padded", "shifted", "prep_stored"))
        iota_done, const_done, vec, turned, copied, zeroed = (sem(n) for n in (
            "iota_done", "const_done", "vec", "turned", "copied", "zeroed"))

        with nc.Block() as block:
            @block.gpsimd
            def _(pool):
                pool.iota(iota_i[:], pattern=[[1, P]], base=0, channel_multiplier=0).then_inc(iota_done, 1)
                pool.iota(part_i[:], pattern=[[0, 1]], base=0, channel_multiplier=1).then_inc(iota_done, 1)
                pool.memset(zeros[:], 0.0).then_inc(zeroed, 1)

            @block.sync
            def _(sp):
                sp.wait_ge(filled, 4)
                for a, b in ((dst, dst_t), (src, src_t), (edge_weight, w_t)):
                    sp.dma_start(b[:, 0:FC, :], a[0:FC * P * P].rearrange("(c p e) -> p c e", p=P, e=P)
                                 ).then_inc(loaded, 16)
                    sp.dma_start(b[0:FR, FC, :], a[FC * P * P:FULL_ROWS * P].rearrange("(p e) -> p e", e=P)
                                 ).then_inc(loaded, 16)
                    sp.dma_start(b[FR:FR + 1, FC, 0:TAIL], a[FULL_ROWS * P:E].rearrange("(p e) -> p e", p=1)
                                 ).then_inc(loaded, 16)
                sp.wait_ge(loaded, 9 * 16)
                sp.dma_start(dst_pad[1:1 + TP * P].rearrange("(c p e) -> p c e", p=P, e=P), dst_t[:]
                             ).then_inc(padded, 16)
                sp.dma_start(dst_pad[0:1].rearrange("(a b) -> a b", a=1), edge_of[:, 0:1]).then_inc(padded, 16)
                sp.dma_start(dst_pad[1 + TP * P:2 + TP * P].rearrange("(a b) -> a b", a=1), edge_of[:, 1:2]
                             ).then_inc(padded, 16)
                sp.wait_ge(padded, 48)
                sp.dma_start(prev_t[:], dst_pad[0:TP * P].rearrange("(c p e) -> p c e", p=P, e=P)
                             ).then_inc(shifted, 16)
                sp.dma_start(next_t[:], dst_pad[2:2 + TP * P].rearrange("(c p e) -> p c e", p=P, e=P)
                             ).then_inc(shifted, 16)
                sp.wait_ge(zeroed, 1)
                for r in range(REPLICAS):
                    table = rel_sum[r].rearrange("n d -> (n d)").rearrange("(z p k) -> z p k", z=4, p=P)
                    for z in range(4):
                        sp.dma_start(table[z], zeros[:]).then_inc(prep_stored, 16)
                sp.wait_ge(vec, 6)
                sp.dma_start(src_flat.rearrange("(c p e) -> p c e", p=P, e=P), srcf_t[:]).then_inc(prep_stored, 16)
                with nc.allow_non_contiguous_dma(reason="one word for each tile, once"):
                    sp.dma_start(starts.rearrange("(c p e) -> p c e", p=P, e=1), start_ti[:]
                                 ).then_inc(prep_stored, 16)
                    sp.dma_start(firsts.rearrange("(c p e) -> p c e", p=P, e=1), dst_t[:, :, 0:1]
                                 ).then_inc(prep_stored, 16)
                sp.wait_ge(vec, 8)
                sp.dma_start(rel_flat.rearrange("(c p e) -> p c e", p=P, e=P), w_t[:]).then_inc(prep_stored, 16)
                sp.wait_ge(vec, 14)
                for m in range(4):
                    sp.dma_start(marks[:, m, :].rearrange("(c p) e -> p c e", p=P), mark_t[:, m]
                                 ).then_inc(prep_stored, 16)
                with nc.allow_non_contiguous_dma(reason="one word for each tile, once"):
                    sp.dma_start(whole[0].rearrange("(c p e) -> p c e", p=P, e=1), mark_t[:, 2, :, P - 1:P]
                                 ).then_inc(prep_stored, 16)
                    sp.dma_start(whole[1].rearrange("(c p e) -> p c e", p=P, e=1), mark_t[:, 3, :, 0:1]
                                 ).then_inc(prep_stored, 16)
                sp.wait_ge(prep_stored, 16 * (4 * REPLICAS + 10))

            @block.vector
            def _(dve):
                nc.vector.memset(src_t[:], 0).then_inc(filled, 1)
                nc.vector.memset(dst_t[:], PAD_DST).then_inc(filled, 1)
                nc.vector.memset(w_t[:], 0.0).then_inc(filled, 1)
                nc.vector.memset(edge_of[:], -1).then_inc(filled, 1)
                dve.wait_ge(iota_done, 2)
                nc.vector.tensor_copy(iota_n[:], iota_i[:]).then_inc(const_done, 1)
                nc.vector.tensor_copy(part[:], part_i[:]).then_inc(const_done, 1)
                dve.wait_ge(const_done, 2)
                nc.vector.tensor_scalar(neg_part[:], part[:], -1.0, None, ALU.mult)
                nc.vector.tensor_scalar(dump_row[:], part[:], float(N), None, ALU.add)
                nc.vector.tensor_scalar(later[:], iota_n[:], part[:, 0:1], None, ALU.is_ge)
                nc.vector.tensor_scalar(ident[:], iota_n[:], part[:, 0:1], None, ALU.is_equal).then_inc(const_done, 1)
                dve.wait_ge(loaded, 9 * 16)
                nc.vector.tensor_copy(srcf_t[:], src_t[:]).then_inc(vec, 1)
                nc.vector.tensor_scalar(start_t[:], dst_t[:, :, 0:1], float(LAST), None, ALU.min).then_inc(vec, 1)
                nc.vector.tensor_scalar(start_ti[:], dst_t[:, :, 0:1], float(LAST), None, ALU.min).then_inc(vec, 1)
                dve.wait_ge(vec, 3)
                nc.vector.tensor_tensor(nrel_t[:], start_t[:].to_broadcast([P, NC, P]), dst_t[:], ALU.subtract
                                        ).then_inc(vec, 1)
                dve.wait_ge(shifted, 32)
                nc.vector.tensor_tensor(mark_t[:, 0], prev_t[:], dst_t[:], ALU.not_equal).then_inc(vec, 1)
                nc.vector.tensor_tensor(mark_t[:, 1], next_t[:], dst_t[:], ALU.not_equal).then_inc(vec, 1)
                dve.wait_ge(vec, 6)
                nc.vector.tensor_scalar(mark_t[:, 0:2], mark_t[:, 0:2], -BIG, None, ALU.mult
                                        ).then_inc(vec, 1)
                dve.wait_ge(copied, NC)
                nc.vector.tensor_scalar(w_t[:], nrel_t[:], -1.0, None, ALU.mult).then_inc(vec, 1)
                dve.wait_ge(vec, 8)
                nc.vector.memset(prev_t[:], 1).then_inc(vec, 1)
                nc.vector.memset(next_t[:], 1).then_inc(vec, 1)
                dve.wait_ge(vec, 10)
                nc.vector.memset(prev_t[:, :, 0:1], 0).then_inc(vec, 1)
                nc.vector.memset(next_t[:, :, P - 1:P], 0).then_inc(vec, 1)
                dve.wait_ge(vec, 12)

                def flat(a):
                    return a.rearrange("p c e -> p (c e)")

                nc.vector.tensor_tensor_scan(flat(mark_t[:, 2]), flat(prev_t[:]), flat(mark_t[:, 0]), 0.0,
                                             ALU.mult, ALU.min).then_inc(vec, 1)
                nc.vector.tensor_tensor_scan(flat(mark_t[:, 3])[:, ::-1], flat(next_t[:])[:, ::-1],
                                             flat(mark_t[:, 1])[:, ::-1], 0.0, ALU.mult, ALU.min).then_inc(vec, 1)

            @block.tensor
            def _(pe):
                pe.wait_ge(const_done, 3)
                pe.wait_ge(vec, 4)
                for c in range(NC):
                    if c >= 2:
                        pe.wait_ge(copied, c - 1)
                    for i, a in enumerate((srcf_t, nrel_t, w_t)):
                        last = nc.tensor.transpose(psum[c % 2][:, i * P:(i + 1) * P], a[:, c, :], ident[:])
                    last.then_inc(turned, 1)

            @block.scalar
            def _(act):
                for c in range(NC):
                    act.wait_ge(turned, c + 1)
                    cols = slice(c * P, (c + 1) * P)
                    for i, a in enumerate((src_col, neg_rel, w_col)):
                        last = nc.scalar.activation(a[:, cols], psum[c % 2][:, i * P:(i + 1) * P], ACT.Copy)
                    last.then_inc(copied, 1)
        with nc.Block() as block:
            @block.vector
            def _(dve):
                nc.vector.tensor_copy(src_t[:].rearrange("p c e -> p (c e)"), src_col[:]).then_inc(vec, 1)

            @block.sync
            def _(sp):
                sp.wait_ge(vec, 15)
                sp.dma_start(src_cols, src_t[:].rearrange("p c e -> p (c e)")).then_inc(padded, 16)
                sp.wait_ge(padded, 64)


def neighbours(nc, e):
    N, D, NG, T, GP, LAST = e["N"], e["D"], e["NG"], e["T"], e["GP"], e["LAST"]
    x, src_flat, starts, rel_sum = e["x"], e["src_flat"], e["starts"], e["rel_sum"]
    iota_n, later, neg_rel, src_col, w_col = e["iota_n"], e["later"], e["neg_rel"], e["src_col"], e["w_col"]
    dump_row, passed = e["dump_row"], e["passed"]
    with ExitStack() as ctx:
        def sb(name, shape, dt=F32):
            return ctx.enter_context(nc.sbuf_tensor(name, shape, dt))

        def sem(name):
            return ctx.enter_context(nc.semaphore(name))

        start_row = sb("start_row", [1, T], I32)
        rel_col = sb("rel_col", [P, T])
        src_bc = sb("src_bc", [P, 2, GP])
        x_win = sb("x_win", [P, 2, G, D])
        same = sb("same", [P, 2, G, P])
        spread = sb("spread", [P, 2, G, P])
        count = sb("count", [P, 2, G])
        to_dump = sb("to_dump", [P, 2, G])
        moved = sb("moved", [P, 2, G])
        row = sb("row", [P, 2, G], I32)
        coef = sb("coef", [P, 2, G, P])
        sums = sb("sums", [P, 2, G, D])
        coef_ps = [ctx.enter_context(nc.psum_tensor(f"coef_ps{i}", [P, 4, P], F32)) for i in range(2)]
        sum_ps = [ctx.enter_context(nc.psum_tensor(f"sum_ps{i}", [P, 4, P], F32)) for i in range(2)]
        starts_in, src_in, x_in = sem("starts_in"), [sem(f"src_in{i}") for i in range(2)], [sem(f"x_in{i}") for i in range(2)]
        rel_ready, masks, rows_a, rows_b, rows = (sem(n) for n in ("rel_ready", "masks", "rows_a", "rows_b", "rows"))
        coef_done, coef_out, sum_done, sum_out = (sem(n) for n in ("coef_done", "coef_out", "sum_done", "sum_out"))
        added = [sem(f"added{r}") for r in range(REPLICAS)]
        PER = G // REPLICAS

        with nc.Block() as block:
            @block.sync
            def _(sp):
                regs = [sp.alloc_register(f"x_start{j}") for j in range(G)]
                sp.dma_start(start_row[:], starts[0:T].rearrange("(a t) -> a t", a=1)).then_inc(starts_in, 16)
                sp.wait_ge(starts_in, 16)

                def body(s):
                    b = s.turn(2)
                    wait(sp, masks, 2 * G * (s.g - 1))
                    sp.dma_start(src_bc[:, b, :], src_flat[bass.ds(s.g * GP, GP)].rearrange("(a e) -> a e", a=1)
                                 .to_broadcast([P, GP])).then_inc(src_in[b], 16)
                    wait_alone(sp, sum_done, 2 * (s.g - 1), passed)
                    start = load_starts(sp, regs, start_row[0:1, bass.ds(s.g * G, G)], LAST)
                    for j in range(G):
                        sp.dma_start(x_win[:, b, j, :], x[bass.ds(start[j], P), :]).then_inc(x_in[b], 16)

                steps(sp, NG, 2, 2, 1, body)

            @block.vector
            def _(dve):
                nc.vector.tensor_scalar(rel_col[:], neg_rel[:, 0:T], -1.0, None, ALU.mult).then_inc(rel_ready, 1)
                dve.wait_ge(rel_ready, 1)

                def body(s):
                    b = s.turn(2)
                    dve.wait_ge(src_in[b], s.uses(2) * 16)
                    wait(dve, coef_done, 2 * (s.g - 1))
                    wait(dve, rows, s.g)
                    for j in range(G):
                        t = bass.ds(s.g * G + j, 1)
                        nc.vector.scalar_tensor_tensor(
                            out=same[:, b, j, :], in0=src_bc[:, b, j * P:(j + 1) * P], scalar=src_col[:, t],
                            in1=later[:], op0=ALU.is_equal, op1=ALU.mult, accum_out=count[:, b, j:j + 1]
                        ).then_inc(masks, 1)
                        nc.vector.tensor_scalar(spread[:, b, j, :], iota_n[:], rel_col[:, t], w_col[:, t],
                                                ALU.is_equal, ALU.mult).then_inc(masks, 1)
                    src8 = src_col[:, bass.ds(s.g * G, G)]
                    nc.vector.tensor_scalar(to_dump[:, b, :], src8, -1.0, dump_row[:, 0:1], ALU.mult, ALU.add
                                            ).then_inc(rows_a, 1)
                    dve.wait_ge(rows_a, s.g + 1)
                    dve.wait_ge(masks, (s.g + 1) * 2 * G)
                    nc.vector.scalar_tensor_tensor(out=moved[:, b, :], in0=count[:, b, :], scalar=1.5,
                                                   in1=to_dump[:, b, :], op0=ALU.is_gt, op1=ALU.mult
                                                   ).then_inc(rows_b, 1)
                    dve.wait_ge(rows_b, s.g + 1)
                    for r in range(REPLICAS):
                        wait(dve, added[r], 16 * PER * (s.g - 1))
                    nc.vector.tensor_tensor(row[:, b, :], moved[:, b, :], src8, ALU.add).then_inc(rows, 1)

                steps(dve, NG, 2, 2, 1, body)

            @block.tensor
            def _(pe):
                def body(s):
                    b = s.turn(2)
                    for k in range(2):
                        wait(pe, coef_out, 2 * s.g - 1 + k)
                        pe.wait_ge(masks, s.g * 2 * G + G * (k + 1))
                        for i in range(4):
                            j = 4 * k + i
                            last = nc.tensor.matmul(coef_ps[k][:, i, :], spread[:, b, j, :], same[:, b, j, :],
                                                    start=True, stop=True)
                        last.then_inc(coef_done, 1)
                    pe.wait_ge(x_in[b], s.uses(2) * 16 * G)
                    for k in range(2):
                        pe.wait_ge(coef_out, s.g * 2 + k + 1)
                        wait(pe, sum_out, 2 * s.g - 1 + k)
                        for i in range(4):
                            j = 4 * k + i
                            last = nc.tensor.matmul(sum_ps[k][:, i, :], coef[:, b, j, :], x_win[:, b, j, :],
                                                    start=True, stop=True)
                        last.then_inc(sum_done, 1)

                steps(pe, NG, 2, 2, 1, body)

            @block.scalar
            def _(act):
                def body(s):
                    b = s.turn(2)
                    for k in range(2):
                        act.wait_ge(coef_done, s.g * 2 + k + 1)
                        wait(act, sum_done, 2 * (s.g - 1))
                        nc.scalar.activation(coef[:, b, 4 * k:4 * k + 4, :], coef_ps[k][:], ACT.Copy
                                             ).then_inc(coef_out, 1)
                    for r in range(REPLICAS):
                        wait(act, added[r], 16 * PER * (s.g - 1))
                    for k in range(2):
                        act.wait_ge(sum_done, s.g * 2 + k + 1)
                        nc.scalar.activation(sums[:, b, 4 * k:4 * k + 4, :], sum_ps[k][:], ACT.Copy
                                             ).then_inc(sum_out, 1)

                steps(act, NG, 2, 2, 1, body)

            @block.gpsimd
            def _(pool):
                def body(s):
                    b = s.turn(2)
                    pool.wait_ge(rows, s.g + 1)
                    for j in range(G):
                        r, before = j % REPLICAS, j // REPLICAS
                        if j % 4 == 0:
                            pool.wait_ge(sum_out, s.g * 2 + j // 4 + 1)
                        wait_alone(pool, added[r], (s.g * PER + before) * 16, passed)
                        pool.indirect_dma_start(
                            out=rel_sum[r], out_offset=bass.IndirectOffsetOnAxis(ap=row[:, b, j:j + 1], axis=0),
                            in_=sums[:, b, j, :], in_offset=None, compute_op=ALU.add,
                            bounds_check=N + P - 1).then_inc(added[r], 16)

                steps(pool, NG, 2, 2, 1, body)
                for r in range(REPLICAS):
                    pool.wait_ge(added[r], 16 * PER * NG)


class Chain:

    def __init__(self, eng, sem, per, i):
        self.eng, self.sem, self.per, self.base, self.n = eng, sem, per, i * per, 0

    def mark(self, ins):
        self.n += 1
        ins.then_inc(self.sem, 1)

    def settle(self):
        self.eng.wait_ge(self.sem, self.base + self.n)

    def link(self, ins):
        self.mark(ins)
        self.settle()

    def close(self):
        assert self.n == self.per, self.n


def layer_norm(nc, ch, i, passed, y, stats, mv, rstd, var_ready, rooted, out, done):
    for j in range(4):
        ch.mark(nc.vector.bn_stats(stats[:, j, :], y[:, j, :]))
    ch.settle()
    ch.eng.sem_inc(passed, 1)
    for j in range(4):
        ch.mark(nc.vector.bn_aggr(mv[:, j, :], stats[:, j, :]))
    ch.settle()
    nc.vector.tensor_scalar(rstd[:, 0, :], mv[:, :, 1], EPS, None, ALU.add).then_inc(var_ready, 1)
    ch.eng.wait_ge(rooted, i + 1)
    ch.link(nc.vector.reciprocal(rstd[:, 2, :], rstd[:, 1, :]))
    for j in range(4):
        nc.vector.tensor_scalar(out[:, j, :], y[:, j, :], mv[:, j, 0:1], rstd[:, 2, j:j + 1],
                                ALU.subtract, ALU.mult).then_inc(done, 1)


def node_steps(eng, N, body):
    full = N // NB
    body(0, 0)
    with eng.Fori(1, full) as i:
        body(i, i * NB)
    body(full, N - NB)


def nodes_one(nc, e):
    N, D = e["N"], e["D"]
    x, rel_sum, x1_rows, q_rows, kv_rows = e["x"], e["rel_sum"], e["x1_rows"], e["q_rows"], e["kv_rows"]
    ident = e["ident"]
    assert N % NB != 0
    with ExitStack() as ctx:
        def sb(name, shape, dt=F32):
            return ctx.enter_context(nc.sbuf_tensor(name, shape, dt))

        def ps(name):
            return ctx.enter_context(nc.psum_tensor(name, [P, 4, P], F32))

        def sem(name):
            return ctx.enter_context(nc.semaphore(name))

        w12 = sb("w12", [P, 2, D])
        wqkv = sb("wqkv", [P, 3, D])
        bias = sb("bias", [P, 4, D])
        xb = sb("xb", [P, 4, D])
        rep = sb("rep", [P, REPLICAS, 4 * D])
        pair = sb("pair", [P, 2, 4, D])
        half_sum = sb("half_sum", [P, 2, 4 * D])
        pair_t = sb("pair_t", [P, 2, 4, P])
        y = sb("y", [P, 4, D])
        stats = sb("stats", [P, 4, 6])
        mv = sb("mv", [P, 4, 2])
        rstd = sb("rstd", [P, 3, 4])
        x1 = sb("x1", [P, 4, D])
        x1_t = sb("x1_t", [P, 4, P])
        qkv = sb("qkv", [P, 4, 3, D])
        pair_ps = [ps("pair_ps0"), ps("pair_ps1")]
        y_ps, x1_ps = ps("y_ps"), ps("x1_ps")
        qkv_ps = [ps(f"qkv_ps{j}") for j in range(4)]
        w_in, bias_ready, in_x, summed, pair_turned, pair_out, y_done = (sem("n1_" + n) for n in (
            "w_in", "bias_ready", "in_x", "summed", "pair_turned", "pair_out", "y_done"))
        var_ready, rooted, x1_ready, x1_turned, x1_out, qkv_done, qkv_ready, stored, ch1 = (sem("n1_" + n) for n in (
            "var_ready", "rooted", "x1_ready", "x1_turned", "x1_out", "qkv_done", "qkv_ready", "stored", "chain"))
        CH = 2 + 1 + 4 + 4 + 1

        with nc.Block() as block:
            @block.sync
            def _(sp):
                for i, w in enumerate((e["W1"], e["W2"])):
                    sp.dma_start(w12[:, i, :], w).then_inc(w_in, 16)
                for i, w in enumerate((e["Wq"], e["Wk"], e["Wv"])):
                    sp.dma_start(wqkv[:, i, :], w).then_inc(w_in, 16)
                for i, b in enumerate((e["bq"], e["bk"], e["bv"], e["be"])):
                    sp.dma_start(bias[:, i, :], b.rearrange("(a d) -> a d", a=1).to_broadcast([P, D])
                                 ).then_inc(w_in, 16)

                def body(i, row0):
                    wait_alone(sp, x1_ready, i * 4, e["passed"])
                    rows = bass.ds(row0, NB)
                    sp.dma_start(xb[:], x[rows, :].rearrange("(p j) d -> p j d", j=4)).then_inc(in_x, 16)
                    for r in range(REPLICAS):
                        sp.dma_start(rep[:, r, :], rel_sum[r][rows, :].rearrange("(p j) d -> p (j d)", j=4)
                                     ).then_inc(in_x, 16)

                node_steps(sp, N, body)

            @block.vector
            def _(dve):
                dve.wait_ge(w_in, 9 * 16)
                nc.vector.tensor_tensor(bias[:, 1, :], bias[:, 1, :], bias[:, 3, :], ALU.add).then_inc(bias_ready, 1)
                dve.wait_ge(bias_ready, 1)

                def body(i, row0):
                    ch = Chain(dve, ch1, CH, i)
                    dve.wait_ge(in_x, (i + 1) * 16 * (1 + REPLICAS))
                    ch.mark(nc.vector.tensor_tensor(half_sum[:, 0, :], rep[:, 0, :], rep[:, 1, :], ALU.add))
                    ch.mark(nc.vector.tensor_tensor(half_sum[:, 1, :], rep[:, 2, :], rep[:, 3, :], ALU.add))
                    ch.settle()
                    wait(dve, pair_turned, i * 2)
                    nc.vector.tensor_tensor(pair[:, 0].rearrange("p j d -> p (j d)"), half_sum[:, 0, :],
                                            half_sum[:, 1, :], ALU.add).then_inc(summed, 1)
                    dve.wait_ge(summed, i * 2 + 1)
                    nc.vector.tensor_tensor(pair[:, 1], pair[:, 0], xb[:], ALU.mult).then_inc(summed, 1)
                    dve.wait_ge(y_done, i + 1)
                    ch.link(nc.vector.tensor_tensor(y[:], xb[:], y_ps[:], ALU.add))
                    wait(dve, stored, i * 48)
                    layer_norm(nc, ch, i, e["passed"], y, stats, mv, rstd, var_ready, rooted, x1, x1_ready)
                    for j in range(4):
                        dve.wait_ge(qkv_done, i * 4 + j + 1)
                        nc.vector.tensor_tensor(qkv[:, j], qkv_ps[j][:, 0:3, :], bias[:, 0:3, :], ALU.add
                                                ).then_inc(qkv_ready, 1)
                    ch.close()

                node_steps(dve, N, body)

            @block.tensor
            def _(pe):
                pe.wait_ge(w_in, 9 * 16)

                def body(i, row0):
                    for k in range(2):
                        pe.wait_ge(summed, i * 2 + k + 1)
                        wait(pe, pair_out, i * 2 - 1 + k)
                        for j in range(4):
                            last = nc.tensor.transpose(pair_ps[k][:, j, :], pair[:, k, j, :], ident[:])
                        last.then_inc(pair_turned, 1)
                    pe.wait_ge(pair_out, i * 2 + 2)
                    for j in range(4):
                        nc.tensor.matmul(y_ps[:, j, :], pair_t[:, 0, j, :], w12[:, 0, :], start=True, stop=False)
                        last = nc.tensor.matmul(y_ps[:, j, :], pair_t[:, 1, j, :], w12[:, 1, :], start=False, stop=True)
                    last.then_inc(y_done, 1)
                    pe.wait_ge(x1_ready, i * 4 + 4)
                    for j in range(4):
                        last = nc.tensor.transpose(x1_ps[:, j, :], x1[:, j, :], ident[:])
                    last.then_inc(x1_turned, 1)
                    pe.wait_ge(x1_out, i + 1)
                    for j in range(4):
                        wait(pe, qkv_ready, i * 4 - 3 + j)
                        nc.tensor.matmul(qkv_ps[j][:, 0:3, :], x1_t[:, j, :], wqkv[:], start=True, stop=True
                                         ).then_inc(qkv_done, 1)

                node_steps(pe, N, body)

            @block.scalar
            def _(act):
                def body(i, row0):
                    for k in range(2):
                        act.wait_ge(pair_turned, i * 2 + k + 1)
                        wait(act, y_done, i)
                        nc.scalar.activation(pair_t[:, k], pair_ps[k][:], ACT.Copy).then_inc(pair_out, 1)
                    act.wait_ge(var_ready, i + 1)
                    nc.scalar.activation(rstd[:, 1, :], rstd[:, 0, :], ACT.Sqrt).then_inc(rooted, 1)
                    act.wait_ge(x1_turned, i + 1)
                    wait(act, qkv_done, i * 4)
                    nc.scalar.activation(x1_t[:], x1_ps[:], ACT.Copy).then_inc(x1_out, 1)

                node_steps(act, N, body)

            @block.gpsimd
            def _(pool):
                def body(i, row0):
                    wait(pool, stored, i * 48)
                    rows = bass.ds(row0, NB)
                    wait_alone(pool, x1_ready, i * 4 + 4, e["passed"])
                    pool.dma_start(x1_rows[rows, :].rearrange("(p j) d -> p j d", j=4), x1[:]).then_inc(stored, 16)
                    wait_alone(pool, qkv_ready, i * 4 + 4, e["passed"])
                    pool.dma_start(q_rows[rows, :].rearrange("(p j) d -> p j d", j=4), qkv[:, :, 0, :]
                                   ).then_inc(stored, 16)
                    pool.dma_start(kv_rows[rows, :].rearrange("(p j) d -> p j d", j=4),
                                   qkv[:, :, 1:3, :].rearrange("p j a d -> p j (a d)")).then_inc(stored, 16)

                node_steps(pool, N, body)
                pool.wait_ge(stored, (N // NB + 1) * 48)


def attention_and_out(nc, e):
    N, D, H, DH, ED = e["N"], e["D"], e["H"], e["DH"], e["ED"]
    NG, T, GP, GH, LAST, E, SCALE = e["NG"], e["T"], e["GP"], e["GH"], e["LAST"], e["E"], e["SCALE"]
    ident, iota_n, part, neg_part, neg_rel = e["ident"], e["iota_n"], e["part"], e["neg_part"], e["neg_rel"]
    with ExitStack() as ctx:
        def sb(name, shape, dt=F32):
            return ctx.enter_context(nc.sbuf_tensor(name, shape, dt))

        def sem(name):
            return ctx.enter_context(nc.semaphore("at_" + name))

        acc = sb("acc", [P, 2, N])
        head_of = sb("head_of", [P, H])
        head_of_t = sb("head_of_t", [H, P])
        row_head = sb("row_head", [GH, H])
        row_head_t = sb("row_head_t", [H, GH])
        row_tile = sb("row_tile", [GH, G])
        attention(nc, e, locals())
        nodes_two(nc, e, acc)


def attention(nc, e, m):
    N, D, H, DH, ED = e["N"], e["D"], e["H"], e["DH"], e["ED"]
    NG, T, GP, GH, LAST, E, SCALE = e["NG"], e["T"], e["GP"], e["GH"], e["LAST"], e["E"], e["SCALE"]
    ident, iota_n, part, neg_part, neg_rel = e["ident"], e["iota_n"], e["part"], e["neg_part"], e["neg_rel"]
    acc, head_of, head_of_t = m["acc"], m["head_of"], m["head_of_t"]
    row_head, row_head_t, row_tile = m["row_head"], m["row_head_t"], m["row_tile"]
    q_rows, kv_rows, edge_attr = e["q_rows"], e["kv_rows"], e["edge_attr"]
    rel_flat, marks, whole, src_cols = e["rel_flat"], e["marks"], e["whole"], e["src_cols"]
    starts, firsts, passed = e["starts"], e["firsts"], e["passed"]
    LONG = (E - (NG - 1) * GP) // P
    SHORT = E - (NG - 1) * GP - LONG * P

    with ExitStack() as ctx:
        def sb(name, shape, dt=F32):
            return ctx.enter_context(nc.sbuf_tensor(name, shape, dt))

        def sem(name):
            return ctx.enter_context(nc.semaphore("at_" + name))

        we2 = sb("we2", [P, 2, D])
        start_row = sb("at_start_row", [1, T], I32)
        first_row = sb("first_row", [1, NG], I32)
        src_idx = sb("src_idx", [P, 3, G], I32)
        kv = sb("kv", [P, 3, G, 2 * D])
        attr = sb("attr", [P, 2, G, ED])
        attr_t = sb("attr_t", [P, G // 2, P])
        rel_bc = sb("rel_bc", [P, 2, GP])
        q_win = sb("q_win", [P, 2, G, D])
        mark = sb("mark", [GH, 2, 4, P])
        whole_row = sb("whole_row", [H, 2, 2, G])
        pick = sb("pick", [P, 2, GP])
        put = sb("put", [P, 2, G, P])
        q_edge = sb("q_edge", [P, GP])
        prod = sb("prod", [P, GP])
        logit = sb("logit", [P, GH])
        fwd = sb("fwd", [GH, P])
        both = sb("both", [GH, P])
        ends = sb("ends", [GH, 2 * G])
        carry = sb("carry", [H, 2, 2 * (G + 1)])
        inflow = sb("inflow", [GH, 2])
        scrap = sb("scrap", [GH, 2 * G])
        peak_a = sb("peak_a", [GH, P])
        peak = sb("peak", [GH, P])
        drop = sb("drop", [H, 1])
        drop_lane = sb("drop_lane", [P, 1])
        decay = sb("decay", [P, 1])
        below = sb("below", [P, GH])
        weight = sb("weight", [P, G, D])
        msg = sb("msg", [P, G, D])
        attr_ps = ctx.enter_context(nc.psum_tensor("attr_ps", [P, G // 2, P], F32))
        ke_ps = [ctx.enter_context(nc.psum_tensor(f"ke_ps{i}", [P, 4, P], F32)) for i in range(2)]
        q_ps = [ctx.enter_context(nc.psum_tensor(f"q_ps{i}", [P, 4, P], F32)) for i in range(2)]
        misc = ctx.enter_context(nc.psum_tensor("misc_ps", [P, 512], F32))
        out_ps = [ctx.enter_context(nc.psum_tensor(f"out_ps{i}", [P, 2, 2, P], F32)) for i in range(2)]
        logit_ps = misc[:, 0:GH]
        turned_ps = misc[0:GH, GH:GH + P]
        peak_ps = misc[:, GH + P:2 * GH + P]
        ends_ps = misc[0:H, 2 * GH + P:2 * GH + P + 2 * G]
        flow_ps = misc[0:GH, 2 * GH + P + 32:2 * GH + P + 32 + 2 * (G + 1)]
        drop_ps = misc[:, 2 * GH + P + 64:2 * GH + P + 65]

        setup_in, c_a, c_b, const_ready, head_t, head_out = (sem(n) for n in (
            "setup_in", "c_a", "c_b", "const_ready", "head_t", "head_out"))
        idx_in, kv_in = [sem(f"idx_in{i}") for i in range(3)], [sem(f"kv_in{i}") for i in range(3)]
        rel_in, attr_in, q_in, mark_in = ([sem(f"{n}{i}") for i in range(2)] for n in (
            "rel_in", "attr_in", "q_in", "mark_in"))
        attr_turned, q_done, ke_done, logit_done, logit_turned, ends_done, flow_done, peak_turned, out_done = (
            sem(n) for n in ("attr_turned", "q_done", "ke_done", "logit_done", "logit_turned", "ends_done", "flow_done",
                             "peak_turned", "out_done"))
        logit_out, attr_out, q_out, decay_ready, weight_ready, pick_dist, pick_ready, put_dist, put_ready = (
            sem(n) for n in ("logit_out", "attr_out", "q_out", "decay_ready", "weight_ready", "pick_dist",
                             "pick_ready", "put_dist", "put_ready"))
        prod_ready, scan, ends_ready, carry_ready, peak_chain, peak_ready, drop_ready, below_ready, msg_ready = (
            sem(n) for n in ("prod_ready", "scan", "ends_ready", "carry_ready", "peak_chain", "peak_ready",
                             "drop_ready", "below_ready", "msg_ready"))
        decayed, summed = sem("decayed"), sem("summed")

        with nc.Block() as block:
            @block.sync
            def _(sp):
                sp.wait_ge(c_b, 2)
                for i in range(2):
                    sp.dma_start(we2[i * ED:(i + 1) * ED, i, :], e["We"]).then_inc(setup_in, 16)
                sp.dma_start(start_row[:], starts[0:T].rearrange("(a t) -> a t", a=1)).then_inc(setup_in, 16)
                with nc.allow_non_contiguous_dma(reason="one word for each group, once"):
                    sp.dma_start(first_row[:], firsts[0:T].rearrange("(a g t) -> a g t", a=1, t=G)[:, :, 0]
                                 ).then_inc(setup_in, 16)
                sp.wait_ge(setup_in, 64)

            @block.gpsimd
            def _(pool):
                def band(t, first, pattern_lo, base_lo, mult_lo, pattern_hi, base_hi, mult_hi):
                    pool.memset(t, 1.0).then_inc(c_a, 1)
                    pool.wait_ge(c_a, 2 * first + 1)
                    pool.affine_select(out=t, in_=t, compare_op=ALU.is_ge, fill=0.0, base=base_lo,
                                       pattern=pattern_lo, channel_multiplier=mult_lo).then_inc(c_a, 1)
                    pool.wait_ge(c_a, 2 * first + 2)
                    pool.affine_select(out=t, in_=t, compare_op=ALU.is_ge, fill=0.0, base=base_hi,
                                       pattern=pattern_hi, channel_multiplier=mult_hi).then_inc(const_ready, 1)

                band(head_of[:], 0, [[-DH, H]], 0, 1, [[DH, H]], DH - 1, -1)
                band(row_tile[:], 1, [[-H, G]], 0, 1, [[H, G]], H - 1, -1)
                pool.memset(acc[:, 0, :], 0.0).then_inc(const_ready, 1)
                pool.memset(carry[:], -BIG).then_inc(const_ready, 1)

            @block.vector
            def _(dve):
                nc.vector.memset(acc[:, 1, :], 0.0)
                nc.vector.memset(we2[:], 0.0).then_inc(c_b, 1)
                nc.vector.tensor_reduce(row_head[:], ident[0:GH, 0:GH].rearrange("p (j h) -> p h j", h=H), AX_X, ALU.add
                                        ).then_inc(c_b, 1)

            @block.tensor
            def _(pe):
                pe.wait_ge(c_b, 2)
                pe.wait_ge(const_ready, 2)
                nc.tensor.transpose(misc[0:H, 0:GH], row_head[:], ident[0:GH, 0:GH]).then_inc(head_t, 1)
                nc.tensor.transpose(misc[0:H, GH:GH + P], head_of[:], ident[:]).then_inc(head_t, 1)

            @block.scalar
            def _(act):
                act.wait_ge(head_t, 2)
                nc.scalar.activation(row_head_t[:], misc[0:H, 0:GH], ACT.Copy)
                nc.scalar.activation(head_of_t[:], misc[0:H, GH:GH + P], ACT.Copy)

        with nc.Block() as block:
            @block.sync
            def _(sp):
                regs = [sp.alloc_register(f"q_start{j}") for j in range(G)]

                def body(n):
                    b, b3 = n.turn(2), n.turn(3)
                    last = not n.before(NG - 1)
                    if not (isinstance(n.u, int) and n.k < 3):
                        sp.wait_ge(kv_in[b3], (n.uses(3) - 1) * 16 * G)
                    sp.dma_start(src_idx[:, b3, :], src_cols[:, bass.ds(n.g * G, G)]).then_inc(idx_in[b3], 16)
                    wait(sp, pick_dist, n.g - 1)
                    sp.dma_start(rel_bc[:, b, :], rel_flat[bass.ds(n.g * GP, GP)].rearrange("(a e) -> a e", a=1)
                                 .to_broadcast([P, GP])).then_inc(rel_in[b], 16)
                    wait(sp, attr_turned, n.g - 1)
                    if last:
                        at = (NG - 1) * GP
                        sp.dma_start(attr[:, b, 0:LONG, :], edge_attr[at:at + LONG * P, :].rearrange(
                            "(j p) f -> p j f", p=P)).then_inc(attr_in[b], 16)
                        sp.dma_start(attr[0:SHORT, b, LONG, :], edge_attr[at + LONG * P:E, :]).then_inc(attr_in[b], 16)
                    else:
                        sp.dma_start(attr[:, b, :, :], edge_attr[bass.ds(n.g * GP, GP), :].rearrange(
                            "(j p) f -> p j f", p=P)).then_inc(attr_in[b], 16)
                    wait_alone(sp, q_done, 2 * (n.g - 1), passed)
                    start = load_starts(sp, regs, start_row[0:1, bass.ds(n.g * G, G)], LAST)
                    for j in range(G):
                        sp.dma_start(q_win[:, b, j, :], q_rows[bass.ds(start[j], P), :]).then_inc(q_in[b], 16)
                    wait(sp, drop_ready, n.g - 1)
                    tile = bass.ds(n.g * G, G)
                    sp.dma_start(mark[:, b, :, :].rearrange("p m e -> p (m e)"),
                                 marks[tile].rearrange("j m e -> j (m e)").rearrange("j (a f) -> j a f", a=1)
                                 .to_broadcast([G, H, 4 * P])).then_inc(mark_in[b], 16)
                    sp.dma_start(whole_row[:, b, :, :], whole[:, tile].rearrange("(a w) j -> a w j", a=1)
                                 .to_broadcast([H, 2, G])).then_inc(mark_in[b], 16)

                steps(sp, NG, 6, 6, (NG - 6) % 6, body)

            @block.gpsimd
            def _(pool):
                def body(n):
                    b3 = n.turn(3)
                    wait_alone(pool, idx_in[b3], n.uses(3) * 16, passed)
                    wait_alone(pool, msg_ready, n.g - 2, passed)
                    for j in range(G):
                        pool.indirect_dma_start(
                            out=kv[:, b3, j, :], out_offset=None, in_=kv_rows,
                            in_offset=bass.IndirectOffsetOnAxis(ap=src_idx[:, b3, j:j + 1], axis=0)
                        ).then_inc(kv_in[b3], 16)

                steps(pool, NG, 6, 6, (NG - 6) % 6, body)

            @block.tensor
            def _(pe):
                def turn_attr(n):
                    b = n.turn(2)
                    last = not n.before(NG - 1)
                    pe.wait_ge(attr_in[b], n.uses(2) * 16 + (16 if last else 0))
                    wait(pe, attr_out, n.g)
                    for i in range(G // 2):
                        mm = nc.tensor.transpose(attr_ps[:, i, :], attr[:, b, 2 * i:2 * i + 2, :].rearrange(
                            "p j f -> p (j f)"), ident[:])
                    mm.then_inc(attr_turned, 1)

                def q_half(n, k):
                    b = n.turn(2)
                    pe.wait_ge(pick_ready, n.g + 1)
                    pe.wait_ge(q_in[b], n.uses(2) * 16 * G)
                    wait(pe, q_out, 2 * n.g - 1 + k)
                    for i in range(4):
                        j = 4 * k + i
                        mm = nc.tensor.matmul(q_ps[k][:, i, :], q_win[:, b, j, :], pick[:, b, j * P:(j + 1) * P],
                                              start=True, stop=True)
                    mm.then_inc(q_done, 1)

                def ke_half(n, k):
                    pe.wait_ge(kv_in[n.turn(3)], n.uses(3) * 16 * G)
                    pe.wait_ge(attr_out, n.g + 1)
                    wait(pe, prod_ready, 2 * n.g - 1 + k)
                    for i in range(4):
                        j = 4 * k + i
                        nc.tensor.matmul(ke_ps[k][:, i, :], kv[:, n.turn(3), j, 0:D], ident[:], start=True,
                                         stop=False, is_transpose=True)
                        mm = nc.tensor.matmul(ke_ps[k][:, i, :], we2[:, j % 2, :], attr_t[:, j // 2, :],
                                              start=False, stop=True)
                    mm.then_inc(ke_done, 1)

                def logits(n):
                    wait(pe, logit_out, n.g)
                    for j in range(G):
                        if j % 4 == 0:
                            pe.wait_ge(prod_ready, 2 * n.g + 1 + j // 4)
                        mm = nc.tensor.matmul(logit_ps[:, j * H:(j + 1) * H], prod[:, j * P:(j + 1) * P], head_of[:],
                                              start=True, stop=True)
                    mm.then_inc(logit_done, 1)

                def turn_logits(n):
                    wait_alone(pe, logit_out, n.g + 1, passed)
                    nc.tensor.transpose(turned_ps, logit[:], ident[:]).then_inc(logit_turned, 1)

                def gather_ends(n):
                    wait_alone(pe, ends_ready, 2 * (n.g + 1), passed)
                    nc.tensor.matmul(ends_ps, row_head[:], ends[:], start=True, stop=True).then_inc(ends_done, 1)

                def spread_carry(n):
                    wait_alone(pe, carry_ready, 3 * (n.g + 1), passed)
                    nc.tensor.matmul(flow_ps, row_head_t[:], carry[:, n.turn(2), :], start=True, stop=True
                                     ).then_inc(flow_done, 1)

                def turn_peak(c):
                    wait_alone(pe, peak_ready, c.g + 1, passed)
                    nc.tensor.transpose(peak_ps, peak[:], ident[0:GH, 0:GH])
                    wait_alone(pe, drop_ready, c.g + 1, passed)
                    nc.tensor.matmul(drop_ps, head_of_t[:], drop[:], start=True, stop=True).then_inc(peak_turned, 1)

                def body(c):
                    n = c.plus(1)
                    more = c.before(NG - 1)
                    if more:
                        turn_attr(n)
                        q_half(n, 0)
                        q_half(n, 1)
                    turn_peak(c)
                    if more:
                        ke_half(n, 0)
                        ke_half(n, 1)
                        logits(n)
                    pe.wait_ge(msg_ready, c.g + 1)
                    pe.wait_ge(put_ready, c.g + 1)
                    pe.wait_ge(weight_ready, c.g + 1)
                    for p2 in range(G // 2):
                        wait(pe, summed, c.g * G + 2 * p2 - 2)
                        for i in range(2):
                            j = 2 * p2 + i
                            nc.tensor.matmul(out_ps[p2 % 2][:, i, 0, :], msg[:, j, :], put[:, c.turn(2), j, :], start=True,
                                             stop=True)
                            mm = nc.tensor.matmul(out_ps[p2 % 2][:, i, 1, :], weight[:, j, :], put[:, c.turn(2), j, :],
                                                  start=True, stop=True)
                        mm.then_inc(out_done, 1)
                        if more and p2 == 0:
                            turn_logits(n)
                        if more and p2 == 2:
                            gather_ends(n)
                        if more and p2 == 3:
                            spread_carry(n)

                zero = Step(0, 0, 6)
                turn_attr(zero)
                q_half(zero, 0)
                q_half(zero, 1)
                ke_half(zero, 0)
                ke_half(zero, 1)
                logits(zero)
                turn_logits(zero)
                gather_ends(zero)
                spread_carry(zero)
                steps(pe, NG, 6, 6, (NG - 6) % 6 + 6, body)

            @block.vector
            def _(dve):
                regs = [dve.alloc_register(f"window{j}") for j in range(G)]
                first_reg = [dve.alloc_register("first_node")]

                def prod_half(n, k):
                    dve.wait_ge(ke_done, 2 * n.g + k + 1)
                    dve.wait_ge(q_out, 2 * n.g + k + 1)
                    wait(dve, logit_done, n.g)
                    cols = slice(k * 4 * P, (k + 1) * 4 * P)
                    nc.vector.tensor_tensor(prod[:, cols], ke_ps[k][:].rearrange("p i e -> p (i e)"), q_edge[:, cols],
                                            ALU.mult).then_inc(prod_ready, 1)

                def scan_forward(c):
                    b = c.turn(2)
                    dve.wait_ge(logit_turned, c.g + 1)
                    dve.wait_ge(mark_in[b], c.uses(2) * 32)
                    nc.vector.tensor_tensor_scan(fwd[:], mark[:, b, 0, :], turned_ps, -BIG, ALU.add, ALU.max
                                                 ).then_inc(scan, 1)

                def scan_back(c):
                    b = c.turn(2)
                    dve.wait_ge(scan, c.g * 3 + 1)
                    nc.vector.tensor_tensor_scan(both[:, ::-1], mark[:, b, 1, ::-1], fwd[:, ::-1], -BIG,
                                                 ALU.add, ALU.max).then_inc(scan, 1)
                    nc.vector.tensor_copy(carry[:, b, 0:1], carry[:, 1 - b, G:G + 1]).then_inc(scan, 1)

                def place_ends(c):
                    dve.wait_ge(scan, c.g * 3 + 3)
                    nc.vector.tensor_scalar(ends[:, 0:G], row_tile[:], fwd[:, P - 1:P], None, ALU.mult
                                            ).then_inc(ends_ready, 1)
                    nc.vector.tensor_scalar(ends[:, G:2 * G], row_tile[:], both[:, 0:1], None, ALU.mult
                                            ).then_inc(ends_ready, 1)

                def carry_over(c):
                    b = c.turn(2)
                    dve.wait_ge(ends_done, c.g + 1)
                    nc.vector.tensor_tensor_scan(carry[:, b, 1:G + 1], whole_row[:, b, 0, :], ends_ps[:, 0:G],
                                                 carry[:, b, 0:1], ALU.add, ALU.max).then_inc(carry_ready, 1)
                    nc.vector.tensor_tensor_scan(carry[:, b, G + 1:2 * G + 1][:, ::-1], whole_row[:, b, 1, ::-1],
                                                 ends_ps[:, G:2 * G][:, ::-1], -BIG, ALU.add, ALU.max
                                                 ).then_inc(carry_ready, 1)
                    nc.vector.memset(carry[:, b, 2 * G + 1:2 * G + 2], -BIG).then_inc(carry_ready, 1)

                def row_inflow(c):
                    dve.wait_ge(flow_done, c.g + 1)
                    nc.vector.tensor_tensor_reduce(
                        out=scrap[:, 0:G], in0=flow_ps[:, 0:G], in1=row_tile[:], scale=1.0, scalar=0.0,
                        op0=ALU.mult, op1=ALU.add, accum_out=inflow[:, 0:1]).then_inc(peak_chain, 1)
                    nc.vector.tensor_tensor_reduce(
                        out=scrap[:, G:2 * G], in0=flow_ps[:, G + 2:2 * G + 2], in1=row_tile[:], scale=1.0,
                        scalar=0.0, op0=ALU.mult, op1=ALU.add, accum_out=inflow[:, 1:2]).then_inc(peak_chain, 1)

                def row_peaks(c):
                    b = c.turn(2)
                    dve.wait_ge(peak_chain, c.g * 3 + 2)
                    nc.vector.scalar_tensor_tensor(out=peak_a[:], in0=mark[:, b, 2, :], scalar=inflow[:, 0:1],
                                                   in1=both[:], op0=ALU.add, op1=ALU.max).then_inc(peak_chain, 1)
                    dve.wait_ge(peak_chain, c.g * 3 + 3)
                    nc.vector.scalar_tensor_tensor(out=peak[:], in0=mark[:, b, 3, :], scalar=inflow[:, 1:2],
                                                   in1=peak_a[:], op0=ALU.add, op1=ALU.max).then_inc(peak_ready, 1)
                    dve.wait_ge(peak_ready, c.g + 1)
                    nc.vector.scalar_tensor_tensor(
                        out=drop[:], in0=carry[:, b, 0:1], scalar=mark[0:H, b, 0, 0:1], in1=peak[0:H, 0:1],
                        op0=ALU.add, op1=ALU.subtract).then_inc(drop_ready, 1)

                between = {0: scan_forward, 1: scan_back, 2: place_ends, 4: carry_over, 6: row_inflow, 7: row_peaks}

                def body(c):
                    b, n = c.turn(2), c.plus(1)
                    more = c.before(NG - 1)
                    dve.wait_ge(peak_turned, c.g + 1)
                    nc.vector.tensor_tensor(below[:], logit[:], peak_ps, ALU.subtract).then_inc(below_ready, 1)
                    nc.vector.tensor_copy(drop_lane[:], drop_ps).then_inc(below_ready, 1)
                    start = load_starts(dve, regs, start_row[0:1, bass.ds(c.g * G, G)], LAST)
                    first, = load_starts(dve, first_reg, first_row[0:1, bass.ds(c.g, 1)], N - 1)
                    if more:
                        prod_half(n, 0)
                        prod_half(n, 1)
                    dve.wait_ge(weight_ready, c.g + 1)
                    wait(dve, out_done, c.g * 4)
                    nc.vector.tensor_tensor(msg[:], kv[:, c.turn(3), :, D:2 * D], weight[:], ALU.mult
                                            ).then_inc(msg_ready, 1)
                    dve.wait_ge(decay_ready, c.g + 1)
                    wait(dve, summed, c.g * G)
                    nc.vector.tensor_scalar(acc[:, :, bass.ds(first, 1)], acc[:, :, bass.ds(first, 1)],
                                            decay[:, 0:1], None, ALU.mult).then_inc(decayed, 1)
                    dve.wait_ge(decayed, c.g + 1)
                    for j in range(G):
                        if j % 2 == 0:
                            dve.wait_ge(out_done, c.g * 4 + j // 2 + 1)
                        if j:
                            dve.wait_ge(summed, c.g * G + j)
                        win = acc[:, :, bass.ds(start[j], P)]
                        nc.vector.tensor_tensor(win, win, out_ps[j // 2 % 2][:, j % 2, :, :], ALU.add
                                                ).then_inc(summed, 1)
                        if more and j in between:
                            between[j](n)

                zero = Step(0, 0, 6)
                prod_half(zero, 0)
                prod_half(zero, 1)
                for stage in (scan_forward, scan_back, place_ends, carry_over, row_inflow, row_peaks):
                    stage(zero)
                steps(dve, NG, 6, 6, (NG - 6) % 6 + 6, body)

            @block.scalar
            def _(act):
                def pick_masks(n):
                    b = n.turn(2)
                    act.wait_ge(rel_in[b], n.uses(2) * 16)
                    wait(act, q_done, 2 * (n.g - 1))
                    nc.scalar.activation(pick[:, b, :], rel_bc[:, b, :], ACT.Abs, bias=neg_part[:, 0:1]
                                         ).then_inc(pick_dist, 1)
                    act.wait_ge(pick_dist, n.g + 1)
                    nc.scalar.activation(pick[:, b, :], pick[:, b, :], ACT.Relu, scale=-1.0, bias=1.0
                                         ).then_inc(pick_ready, 1)

                def logit_copy(n):
                    act.wait_ge(logit_done, n.g + 1)
                    wait(act, below_ready, 2 * n.g)
                    nc.scalar.activation(logit[:], logit_ps, ACT.Copy).then_inc(logit_out, 1)

                def put_masks(n):
                    wait(act, out_done, 4 * (n.g - 1))
                    for j in range(G):
                        nc.scalar.activation(put[:, n.turn(2), j, :], iota_n[:], ACT.Abs,
                                             bias=neg_rel[:, bass.ds(n.g * G + j, 1)]).then_inc(put_dist, 1)
                    act.wait_ge(put_dist, (n.g + 1) * G)
                    nc.scalar.activation(put[:, n.turn(2)], put[:, n.turn(2)], ACT.Relu, scale=-1.0, bias=1.0
                                         ).then_inc(put_ready, 1)

                def attr_copy(n):
                    act.wait_ge(attr_turned, n.g + 1)
                    wait(act, ke_done, 2 * n.g)
                    nc.scalar.activation(attr_t[:], attr_ps[:], ACT.Copy).then_inc(attr_out, 1)

                def q_copy(n, k):
                    act.wait_ge(q_done, 2 * n.g + k + 1)
                    wait(act, prod_ready, 2 * n.g - 1 + k)
                    nc.scalar.activation(q_edge[:, k * 4 * P:(k + 1) * 4 * P],
                                         q_ps[k][:].rearrange("p i e -> p (i e)"), ACT.Copy).then_inc(q_out, 1)

                def body(c):
                    n = c.plus(1)
                    more = c.before(NG - 1)
                    if more:
                        attr_copy(n)
                        q_copy(n, 0)
                        q_copy(n, 1)
                    act.wait_ge(below_ready, 2 * (c.g + 1))
                    wait(act, decayed, c.g)
                    nc.scalar.activation(decay[:], drop_lane[:], ACT.Exp, scale=SCALE).then_inc(decay_ready, 1)
                    wait(act, out_done, c.g * 4)
                    nc.scalar.activation(weight[:].rearrange("p j (h d) -> p (j h) d", d=DH),
                                         below[:].rearrange("p (r a) -> p r a", a=1).to_broadcast([P, GH, DH]),
                                         ACT.Exp, scale=SCALE).then_inc(weight_ready, 1)
                    if c.before(NG - 2):
                        pick_masks(c.plus(2))
                    if more:
                        logit_copy(n)
                        put_masks(n)

                zero = Step(0, 0, 6)
                pick_masks(zero)
                pick_masks(zero.plus(1))
                put_masks(zero)
                attr_copy(zero)
                q_copy(zero, 0)
                q_copy(zero, 1)
                logit_copy(zero)
                steps(act, NG, 6, 6, (NG - 6) % 6 + 6, body)


def nodes_two(nc, e, acc):
    N, D, x1_rows, out = e["N"], e["D"], e["x1_rows"], e["out"]
    with ExitStack() as ctx:
        def sb(name, shape, dt=F32):
            return ctx.enter_context(nc.sbuf_tensor("n2_" + name, shape, dt))

        def sem(name):
            return ctx.enter_context(nc.semaphore("n2_" + name))

        wo = sb("wo", [P, D])
        bo = sb("bo", [P, D])
        xb = sb("xb", [P, 4, D])
        inv = sb("inv", [P, NB])
        att = sb("att", [P, NB])
        xo = sb("xo", [P, 4, D])
        y = sb("y", [P, 4, D])
        stats = sb("stats", [P, 4, 6])
        mv = sb("mv", [P, 4, 2])
        rstd = sb("rstd", [P, 3, 4])
        res = sb("res", [P, 4, D])
        y_ps = ctx.enter_context(nc.psum_tensor("n2_y_ps", [P, 4, P], F32))
        w_in, in_x, att_ready, y_done, y_read, var_ready, rooted, res_ready, stored, chain = (sem(n) for n in (
            "w_in", "in_x", "att_ready", "y_done", "y_read", "var_ready", "rooted", "res_ready", "stored", "chain"))
        CH = 1 + 1 + 4 + 4 + 1

        with nc.Block() as block:
            @block.sync
            def _(sp):
                sp.dma_start(wo[:], e["Wo"]).then_inc(w_in, 16)
                sp.dma_start(bo[:], e["bo"].rearrange("(a d) -> a d", a=1).to_broadcast([P, D])).then_inc(w_in, 16)

                def body(i, row0):
                    wait(sp, y_read, i)
                    sp.dma_start(xb[:], x1_rows[bass.ds(row0, NB), :].rearrange("(p j) d -> p j d", j=4)
                                 ).then_inc(in_x, 16)

                node_steps(sp, N, body)

            @block.vector
            def _(dve):
                dve.wait_ge(w_in, 32)

                def body(i, row0):
                    ch = Chain(dve, chain, CH, i)
                    nodes = bass.ds(row0, NB)
                    ch.link(nc.vector.reciprocal(inv[:], acc[:, 1, nodes]))
                    wait(dve, y_done, i)
                    nc.vector.tensor_tensor(att[:], acc[:, 0, nodes], inv[:], ALU.mult).then_inc(att_ready, 1)
                    dve.wait_ge(in_x, (i + 1) * 16)
                    nc.vector.tensor_tensor(xo[:], xb[:], bo[:].rearrange("p (a d) -> p a d", a=1)
                                            .to_broadcast([P, 4, D]), ALU.add).then_inc(y_read, 1)
                    dve.wait_ge(y_read, i + 1)
                    dve.wait_ge(y_done, i + 1)
                    ch.link(nc.vector.tensor_tensor(y[:], xo[:], y_ps[:], ALU.add))
                    wait(dve, stored, i * 16)
                    layer_norm(nc, ch, i, e["passed"], y, stats, mv, rstd, var_ready, rooted, res, res_ready)
                    ch.close()

                node_steps(dve, N, body)

            @block.tensor
            def _(pe):
                pe.wait_ge(w_in, 32)

                def body(i, row0):
                    pe.wait_ge(att_ready, i + 1)
                    wait(pe, var_ready, i)
                    rows = att[:].rearrange("l (p j) -> l j p", j=4)
                    for j in range(4):
                        mm = nc.tensor.matmul(y_ps[:, j, :], rows[:, j, :], wo[:], start=True, stop=True)
                    mm.then_inc(y_done, 1)

                node_steps(pe, N, body)

            @block.scalar
            def _(act):
                def body(i, row0):
                    act.wait_ge(var_ready, i + 1)
                    nc.scalar.activation(rstd[:, 1, :], rstd[:, 0, :], ACT.Sqrt).then_inc(rooted, 1)

                node_steps(act, N, body)

            @block.gpsimd
            def _(pool):
                def body(i, row0):
                    pool.wait_ge(res_ready, (i + 1) * 4)
                    wait_alone(pool, stored, i * 16, e["passed"])
                    pool.dma_start(out[bass.ds(row0, NB), :].rearrange("(p j) d -> p j d", j=4), res[:]
                                   ).then_inc(stored, 16)

                node_steps(pool, N, body)
                pool.wait_ge(stored, (N // NB + 1) * 16)


_INS = ["x", "src", "dst", "edge_attr_64", "edge_weight", "L0_gnn_W1", "L0_gnn_W2", "L1_gnn_Wq", "L1_gnn_bq",
        "L1_gnn_Wk", "L1_gnn_bk", "L1_gnn_Wv", "L1_gnn_bv", "L1_gnn_We", "L1_gnn_be", "L1_gnn_Wo", "L1_gnn_bo"]


def kernel(**inputs):
    import numpy as np
    import concourse.bacc as bacc
    from concourse.bass_utils import run_bass_kernel_spmd

    nc = bacc.Bacc("TRN2", target_bir_lowering=False, num_devices=1)
    arrays, args = {}, []
    for name in _INS:
        a = np.ascontiguousarray(inputs[name])
        arrays[f"in_{name}"] = a
        args.append(nc.dram_tensor(f"in_{name}", a.shape, mybir.dt.from_np(a.dtype), kind="ExternalInput").ap())
    out = nc.dram_tensor("out", inputs["x"].shape, F32, kind="ExternalOutput").ap()
    build_gnn(nc, *args, out)
    r = run_bass_kernel_spmd(nc, [arrays], core_ids=[0])
    return r.results[0]["out"]
```
